# Optimizing a Trainium2 kernel written in Bass

```python
import numpy as np
import jax
import jax.numpy as jnp

def _softmax(x, axis=-1):
    return jax.nn.softmax(x, axis=axis)

def _gelu(x):
    return jax.nn.gelu(x, approximate=True)

def _silu(x):
    return jax.nn.silu(x)

def _sigmoid(x):
    return jax.nn.sigmoid(x)

def _layernorm(x, axis=-1, eps=1e-05):
    m = jnp.mean(x, axis=axis, keepdims=True)
    v = jnp.var(x, axis=axis, keepdims=True)
    return (x - m) / jnp.sqrt(v + eps)

def _scatter_add(tgt, idx, src, axis=0):
    return tgt.at[idx].add(src)

def _segment_sum(src, seg, n):
    return jax.ops.segment_sum(src, seg, n)
kernel_name = 'mk_adj_resnorm_d2_adj_r2_c252f6'

def setup_inputs(seed: int=0):
    np.random.seed(seed)
    _w = jnp.asarray

    def _rec_inputs():
        import jax
        import jax.numpy as jnp
        _gk = jax.random.key(seed)
        x = -0.001547 + 1.001 * jax.random.normal(jax.random.fold_in(_gk, 1), (128, 128, 128), jnp.float32)
        _w = (1.0 + jnp.arange(128, dtype=jnp.float32)) ** (-0.5)
        _w = _w / _w.mean()
        _pij = jnp.clip(0.125 * _w[:, None] * _w[None, :], 0.0, 1.0)
        _a = jax.random.uniform(jax.random.fold_in(_gk, 2), (128, 128, 128)) < _pij
        _a = jnp.logical_or(_a, jnp.eye(128, dtype=bool))
        adj = _a.astype(jnp.int32)
        _nm = jnp.ones((128, 128), dtype=bool)
        nodemask = jnp.where(_nm, 1.0, 0.0).astype(jnp.float32)
        return (x, adj, nodemask)
    x, adj, nodemask = _rec_inputs()

    def _L0_gnn_setup():
        import jax, jax.numpy as jnp
        import numpy as np
        D_MODEL = 128
        NUM_REL = 40

        def _direction(x, W, Wg, b, bg, adj, rel_ids):
            h = x @ W.T
            g = h @ Wg.T
            vals = (h[:, :, None, :] + b) * jax.nn.sigmoid(g[:, :, None, :] + bg)
            onehot = (adj[..., None] == rel_ids).astype(h.dtype)
            return jnp.einsum('bnmr,bmrd->bnd', onehot, vals)
        key = jax.random.key(seed)
        ks = jax.random.split(key, 16)
        B, N, d = (2, 256, D_MODEL)
        s = 0.02
        inp = {'node': jax.random.normal(ks[0], (B, N, d), dtype=jnp.float32), 'node_mask': jnp.ones((B, N), dtype=jnp.float32), 'adj_mat': jax.random.randint(ks[1], (B, N, N), 0, 41, dtype=jnp.int32), 'W_fwd': jax.random.normal(ks[2], (d, d), dtype=jnp.float32) * s, 'W_bwd': jax.random.normal(ks[3], (d, d), dtype=jnp.float32) * s, 'W_loop': jax.random.normal(ks[4], (d, d), dtype=jnp.float32) * s, 'Wg_fwd': jax.random.normal(ks[5], (d, d), dtype=jnp.float32) * s, 'Wg_bwd': jax.random.normal(ks[6], (d, d), dtype=jnp.float32) * s, 'Wg_loop': jax.random.normal(ks[7], (d, d), dtype=jnp.float32) * s, 'b_fwd': jax.random.normal(ks[8], (NUM_REL - 1, d), dtype=jnp.float32) * s, 'b_bwd': jax.random.normal(ks[9], (NUM_REL - 1, d), dtype=jnp.float32) * s, 'b_loop': jax.random.normal(ks[10], (1, d), dtype=jnp.float32) * s, 'bg_fwd': jax.random.normal(ks[11], (NUM_REL - 1, d), dtype=jnp.float32) * s, 'bg_bwd': jax.random.normal(ks[12], (NUM_REL - 1, d), dtype=jnp.float32) * s, 'bg_loop': jax.random.normal(ks[13], (1, d), dtype=jnp.float32) * s}
        return inp
    _L0_gnn_all = _L0_gnn_setup()
    _L0_gnn_in = {k: v for k, v in _L0_gnn_all.items() if k in ('W_fwd', 'W_bwd', 'W_loop', 'Wg_fwd', 'Wg_bwd', 'Wg_loop', 'b_fwd', 'b_bwd', 'b_loop', 'bg_fwd', 'bg_bwd', 'bg_loop')}
    del _L0_gnn_all

    def _L1_gnn_setup():
        import jax, jax.numpy as jnp
        import numpy as np
        B, N, D_IN, D_OUT, R = (8, 1024, 128, 128, 4)
        key = jax.random.key(seed)
        k1, k2, k3, k4 = jax.random.split(key, 4)
        x = jax.random.normal(k1, (B, N, D_IN), dtype=jnp.float32)
        adj = jnp.zeros((1,), dtype=jnp.float32)
        relation = jax.random.randint(k2, (B, N, N), 0, R + 1, dtype=jnp.int32)
        weight = jax.random.normal(k3, (R, D_IN, D_OUT), dtype=jnp.float32) * 0.05
        bias = jax.random.normal(k4, (D_OUT,), dtype=jnp.float32) * 0.05
        return {'x': x, 'adj': adj, 'relation': relation, 'weight': weight, 'bias': bias}
    _L1_gnn_all = _L1_gnn_setup()
    _L1_gnn_in = {k: v for k, v in _L1_gnn_all.items() if k in ('adj', 'weight', 'bias')}
    del _L1_gnn_all
    return {'x': x, 'adj': adj, 'nodemask': nodemask, 'L0_gnn_W_fwd': _L0_gnn_in['W_fwd'], 'L0_gnn_W_bwd': _L0_gnn_in['W_bwd'], 'L0_gnn_W_loop': _L0_gnn_in['W_loop'], 'L0_gnn_Wg_fwd': _L0_gnn_in['Wg_fwd'], 'L0_gnn_Wg_bwd': _L0_gnn_in['Wg_bwd'], 'L0_gnn_Wg_loop': _L0_gnn_in['Wg_loop'], 'L0_gnn_b_fwd': _L0_gnn_in['b_fwd'], 'L0_gnn_b_bwd': _L0_gnn_in['b_bwd'], 'L0_gnn_b_loop': _L0_gnn_in['b_loop'], 'L0_gnn_bg_fwd': _L0_gnn_in['bg_fwd'], 'L0_gnn_bg_bwd': _L0_gnn_in['bg_bwd'], 'L0_gnn_bg_loop': _L0_gnn_in['bg_loop'], 'L1_gnn_adj': _L1_gnn_in['adj'], 'L1_gnn_weight': _L1_gnn_in['weight'], 'L1_gnn_bias': _L1_gnn_in['bias']}

def reference(x, adj, nodemask, L0_gnn_W_fwd, L0_gnn_W_bwd, L0_gnn_W_loop, L0_gnn_Wg_fwd, L0_gnn_Wg_bwd, L0_gnn_Wg_loop, L0_gnn_b_fwd, L0_gnn_b_bwd, L0_gnn_b_loop, L0_gnn_bg_fwd, L0_gnn_bg_bwd, L0_gnn_bg_loop, L1_gnn_adj, L1_gnn_weight, L1_gnn_bias):
    import jax
    import jax.numpy as jnp

    def _L0_gnn_ref(node, node_mask, adj_mat, W_fwd, W_bwd, W_loop, Wg_fwd, Wg_bwd, Wg_loop, b_fwd, b_bwd, b_loop, bg_fwd, bg_bwd, bg_loop):
        import jax, jax.numpy as jnp
        import numpy as np
        D_MODEL = 128
        NUM_REL = 40

        def _direction(x, W, Wg, b, bg, adj, rel_ids):
            h = x @ W.T
            g = h @ Wg.T
            vals = (h[:, :, None, :] + b) * jax.nn.sigmoid(g[:, :, None, :] + bg)
            onehot = (adj[..., None] == rel_ids).astype(h.dtype)
            return jnp.einsum('bnmr,bmrd->bnd', onehot, vals)
        rels = jnp.arange(2, NUM_REL + 1, dtype=adj_mat.dtype)
        rel1 = jnp.array([1], dtype=adj_mat.dtype)
        adj_t = jnp.swapaxes(adj_mat, -1, -2)
        out = _direction(node, W_fwd, Wg_fwd, b_fwd, bg_fwd, adj_mat, rels)
        out = out + _direction(node, W_bwd, Wg_bwd, b_bwd, bg_bwd, adj_t, rels)
        out = out + _direction(node, W_loop, Wg_loop, b_loop, bg_loop, adj_t, rel1)
        return jax.nn.relu(out)

    def _L1_gnn_ref(x, adj, relation, weight, bias):
        import jax, jax.numpy as jnp
        import numpy as np
        B, N, D_IN, D_OUT, R = (8, 1024, 128, 128, 4)
        rel_ids = jnp.arange(1, weight.shape[0] + 1, dtype=relation.dtype)
        masks = (relation[None] == rel_ids[:, None, None, None]).astype(x.dtype)
        h = jnp.einsum('rbnm,bmd->rbnd', masks, x)
        y = jnp.einsum('rbnd,rdo->bno', h, weight)
        return y + bias
    x = _layernorm(x + _L0_gnn_ref(x, nodemask, adj, L0_gnn_W_fwd, L0_gnn_W_bwd, L0_gnn_W_loop, L0_gnn_Wg_fwd, L0_gnn_Wg_bwd, L0_gnn_Wg_loop, L0_gnn_b_fwd, L0_gnn_b_bwd, L0_gnn_b_loop, L0_gnn_bg_fwd, L0_gnn_bg_bwd, L0_gnn_bg_loop), axis=-1)
    x = _layernorm(x + _L1_gnn_ref(x, L1_gnn_adj, adj, L1_gnn_weight, L1_gnn_bias), axis=-1)
    return x

_drawn_inputs = setup_inputs


def setup_inputs(seed=0):
    import zlib

    import numpy as np

    out = dict(_drawn_inputs(seed))
    spreads = {}
    factors = {'L0_gnn_Wg_loop': 2.808, 'L0_gnn_bg_loop': 6.472, 'L1_gnn_bias': 2.856}
    for name, (base, spread) in spreads.items():
        noise = np.random.default_rng([zlib.crc32(name.encode()), seed]).standard_normal(out[name].shape)
        drawn = base * np.exp(spread * noise) if base else spread * noise
        out[name] = jnp.asarray(drawn.astype(out[name].dtype))
    for name, factor in factors.items():
        out[name] = (out[name] * factor).astype(out[name].dtype)
    return out
```

```python
from collections import namedtuple
from contextlib import ExitStack

import concourse.bass as bass
from concourse import mybir

F32 = mybir.dt.float32
F32R = mybir.dt.float32r
I32 = mybir.dt.int32
BF16 = mybir.dt.bfloat16
ALU = mybir.AluOpType
ACT = mybir.ActivationFunctionType
AX_X = mybir.AxisListType.X

P = 128
B = 128
GB = 4
GROUPS = B // GB
RING = 4
W = GB * P
HALF = W // 2
EPS = 1e-5
RSQRT_MAGIC = float(0x5F3759DF)
NEWTON = 3


LAG_GATE, LAG_LOOP, LAG_NORM1, LAG_MSG, LAG_PROJ, LAG_NORM2 = 0, 1, 4, 6, 7, 10
SLOTS = GROUPS + LAG_NORM2
FIRST_STATS = 3
FULL = RING * -(-LAG_NORM2 // RING)
STAT_OPS = 8 + 3 * NEWTON

RELS = 39
MSGS = 4
FWD, BWD, LOOP = range(3)
CHAIN = 2 * (1 + 5 + 3 * NEWTON)


class Group(namedtuple("Group", "period offset")):

    def back(self, n):
        return Group(self.period, self.offset - n)

    @property
    def spot(self):
        return self.offset % RING

    @property
    def turn(self):
        return self.period + self.offset // RING

    @property
    def number(self):
        return self.period * RING + self.offset

    @property
    def count(self):
        return min(self.number + 1, GROUPS) if self.fixed else self.number + 1

    @property
    def pair(self):
        return self.period * (RING // 2) + self.offset // 2

    @property
    def fixed(self):
        return isinstance(self.period, int)

    def exists(self):
        return not self.fixed or 0 <= self.number < GROUPS


def await_count(eng, sem, count):
    if not isinstance(count, int) or count > 0:
        eng.wait_ge(sem, count)


def run_slots(eng, slot):
    full = FULL
    for t in range(full):
        slot(Group(t // RING, t % RING))
    with eng.Fori(full // RING, GROUPS // RING) as period:
        for j in range(RING):
            slot(Group(period, j))
    for t in range(GROUPS, SLOTS):
        slot(Group(t // RING, t % RING))


def build(nc, x, x_t, adj, adj_t, w_in, w_loop_t, wg_loop_t, biases, w_msg,
          w_rel_t, wg_rel_t, b_rel, bg_rel, w_msgs, rel_ids, identity, out):
    with ExitStack() as ctx:
        def sb(name, shape, dt):
            return ctx.enter_context(nc.sbuf_tensor(name, shape, dt))

        def sem(name):
            return ctx.enter_context(nc.semaphore(name))

        x_sb = sb("x_sb", [P, RING, W], F32)
        xt_sb = sb("xt_sb", [P, RING, W], F32)
        adj_sb = sb("adj_sb", [P, RING, W], F32)
        adjt_sb = sb("adjt_sb", [P, RING, W], F32)
        gate = sb("gate", [P, 2, W], F32)
        vals = sb("vals", [P, 2, W], F32)
        s_sb = sb("s_sb", [P, RING, W], F32)
        x1 = sb("x1", [P, RING, W], F32)
        msg_t = sb("msg_t", [P, 2, W], F32)
        z_sb = sb("z_sb", [P, RING, W], F32)
        out_sb = sb("out_sb", [P, RING, W], F32)
        ticket = sb("ticket", [P, 1 + RING], F32)
        half = sb("half", [P, 1], F32)
        seen = sb("seen", [P, 2 * W], BF16)
        seen_sum = sb("seen_sum", [P, GROUPS // 2], F32)

        stats = sb("stats", [P, 2, 2, 2 * GB, 6], F32)
        rstd = sb("rstd", [P, 2, 2, 2 * GB], F32)
        nmr = sb("nmr", [P, 2, 2, 2 * GB], F32)
        tiny = sb("tiny", [P, 8, 2, 2 * GB], F32)

        w_gate = sb("w_gate", [P, 2 * P], F32)
        w_loop = sb("w_loop", [P, P], F32)
        wg_t = sb("wg_t", [P, P], F32)
        w1 = sb("w1", [P, P], F32)
        b_rows = sb("b_rows", [P, 2, W], F32)
        b_split = sb("b_split", [P, 2, W], F32R)
        pick = sb("pick", [P, P], F32)
        pick_r = sb("pick_r", [P, P], F32R)

        gw_t = sb("gw_t", [P, 3, P], F32)
        gwg_t = sb("gwg_t", [P, 3, P], F32)
        gb = sb("gb", [P, 2 * RELS + 1], F32)
        gbg = sb("gbg", [P, 2 * RELS + 1], F32)
        gw_msg = sb("gw_msg", [P, MSGS, P], F32)
        gids = sb("gids", [P, RELS], F32)
        ident = sb("ident", [P, P], F32)
        gh = sb("gh", [P, 3, W], F32)
        gg = sb("gg", [P, 2, W], F32)
        ggate = sb("ggate", [P, 2, W], F32)
        gvals_t = sb("gvals_t", [P, 2, W], F32)
        gvals = sb("gvals", [P, 2, W], F32)
        gmask = sb("gmask", [P, MSGS, W], F32)
        gsum = sb("gsum", [P, W], F32)
        gx1 = sb("gx1", [P, W], F32)
        gmsg = sb("gmsg", [P, MSGS, W], F32)
        gstat = sb("gstat", [P, GB, 6], F32)
        gmv = sb("gmv", [P, GB, 2], F32)
        gtiny = sb("gtiny", [P, 4, GB], F32)
        worst = sb("worst", [P, 1], F32)
        odd = sb("odd", [P, 1], F32)
        ones = sb("ones", [P, 1], F32)
        flag = sb("flag", [1, 1], I32)

        hg_ps = ctx.enter_context(nc.psum_tensor("hg_ps", [P, 2, GB, 2 * P], F32))
        loop_ps = ctx.enter_context(nc.psum_tensor("loop_ps", [P, 2, W], F32))
        msg_ps = ctx.enter_context(nc.psum_tensor("msg_ps", [P, W], F32))
        y_ps = ctx.enter_context(nc.psum_tensor("y_ps", [P, W], F32))

        x_in = [sem(f"x_in{j}") for j in range(RING)]
        xt_in = [sem(f"xt_in{j}") for j in range(RING)]
        adj_in = [sem(f"adj_in{j}") for j in range(2)]
        adjt_in = [sem(f"adjt_in{j}") for j in range(2)]
        out_st = [sem(f"out_st{j}") for j in range(RING)]
        w_in_sem = sem("w_in_sem")
        fold_in = sem("fold_in")
        bias_in = sem("bias_in")
        cleared = sem("cleared")
        ticket_ready = sem("ticket_ready")
        const_ready = sem("const_ready")
        fold_done = sem("fold_done")
        weights_ready = sem("weights_ready")
        hg_done = sem("hg_done")
        gate_done = sem("gate_done")
        vals_done = sem("vals_done")
        loop_done = sem("loop_done")
        s_done = sem("s_done")
        bn1_done = sem("bn1_done")
        bn2_done = sem("bn2_done")
        tiny_done = sem("tiny_done")
        x1_done = sem("x1_done")
        msg_done = sem("msg_done")
        msgt_done = sem("msgt_done")
        y_done = sem("y_done")
        z_done = sem("z_done")
        out_done = sem("out_done")
        seen_done = sem("seen_done")

        odd_ready = sem("odd_ready")
        odd_count = sem("odd_count")
        flag_ready = sem("flag_ready")
        gw_in = sem("gw_in")
        gx_in = sem("gx_in")
        gadj_in = sem("gadj_in")
        gh_done = sem("gh_done")
        gh_copied = sem("gh_copied")
        gg_done = sem("gg_done")
        gg_copied = sem("gg_copied")
        rel_gates = sem("rel_gates")
        rel_vals = sem("rel_vals")
        rel_turned = sem("rel_turned")
        rel_copied = sem("rel_copied")
        rel_product = sem("rel_product")
        rel_added = sem("rel_added")
        gchain = sem("gchain")
        gmasks_ready = sem("gmasks_ready")
        gmsg_done = sem("gmsg_done")
        gmsg_copied = sem("gmsg_copied")
        gy_done = sem("gy_done")
        gout_ready = sem("gout_ready")
        gout_st = sem("gout_st")

        bank = [hg_ps[:, k // 2, 2 * (k % 2):2 * (k % 2) + 2, :].rearrange("p a n -> p (a n)") for k in range(4)]

        def general(eng, steps, stores=()):
            eng.wait_ge(flag_ready, 1)
            found = eng.value_load(flag[0:1, 0:1], min_val=0, max_val=P)
            with eng.If(found > 0):
                for j in range(RING):
                    eng.wait_ge(out_st[j], 16 * GROUPS // RING)
                eng.wait_ge(gw_in, 16 * 7)
                with eng.Fori(0, GROUPS // 2) as pair:
                    steps(pair)
                for store in stores:
                    eng.wait_ge(store, 16 * GROUPS)

        block = ctx.enter_context(nc.Block())

        def batch(b):
            return slice(b * P, (b + 1) * P)

        @block.sync
        def _(sp):
            def load_xt(q):
                if q.exists():
                    await_count(sp, hg_done, q.number - RING + 1)
                    sp.dma_start(xt_sb[:, q.spot, :], x_t[bass.ds(q.number, 1)].rearrange("o p n -> p (o n)"))\
                        .then_inc(xt_in[q.spot], 16)

            def load_x(q):
                if q.exists():
                    await_count(sp, s_done, q.number - RING + 1)
                    sp.dma_start(x_sb[:, q.spot, :], x[bass.ds(q.number, 1)].rearrange("o p n -> p (o n)"))\
                        .then_inc(x_in[q.spot], 16)

            sp.dma_start(w_loop[:, :], w_in).then_inc(fold_in, 16)
            sp.dma_start(wg_t[:, :], wg_loop_t).then_inc(fold_in, 16)
            sp.wait_ge(cleared, 1)
            for row in (0, 32):
                sp.dma_start(b_rows[row:row + 1, :, :], biases).then_inc(bias_in, 16)
            load_xt(Group(0, 0))
            sp.dma_start(w_gate[:, 0:P], w_loop_t).then_inc(w_in_sem, 16)
            sp.dma_start(w1[:, :], w_msg).then_inc(w_in_sem, 16)
            load_xt(Group(0, 1))
            load_xt(Group(0, 2))
            load_x(Group(0, 0))
            load_x(Group(0, 1))
            sp.dma_start(gw_t[:, :, :], w_rel_t).then_inc(gw_in, 16)
            sp.dma_start(gwg_t[:, :, :], wg_rel_t).then_inc(gw_in, 16)
            sp.dma_start(gb[:, :], b_rel).then_inc(gw_in, 16)
            sp.dma_start(gbg[:, :], bg_rel).then_inc(gw_in, 16)
            sp.dma_start(gw_msg[:, :, :], w_msgs).then_inc(gw_in, 16)
            sp.dma_start(gids[:, :], rel_ids).then_inc(gw_in, 16)
            sp.dma_start(ident[:, :], identity).then_inc(gw_in, 16)

            def slot(t):
                if not t.fixed or t.number + 3 < GROUPS:
                    load_xt(t.back(-3))
                if not t.fixed or t.number + 2 < GROUPS:
                    load_x(t.back(-2))
                q = t.back(LAG_NORM2)
                if q.exists():
                    sp.wait_ge(out_done, q.number + 1)
                    sp.dma_start(out[bass.ds(q.number, 1)].rearrange("o p n -> p (o n)"), out_sb[:, q.spot, :])\
                        .then_inc(out_st[q.spot], 16)

            full = FULL
            for t in range(full):
                slot(Group(t // RING, t % RING))
            with sp.Fori(full // RING, GROUPS // RING - 1) as period:
                for j in range(RING):
                    slot(Group(period, j))
            for t in range(GROUPS - RING, SLOTS):
                slot(Group(t // RING, t % RING))
            for j in range(RING):
                sp.wait_ge(out_st[j], 16 * GROUPS // RING)

            def general_pair(pair):
                for half in range(2):
                    g = pair * 2 + half
                    sp.dma_start(x_sb[:, 0, :], x[bass.ds(g, 1)].rearrange("o p n -> p (o n)")).then_inc(gx_in, 16)
                    sp.dma_start(xt_sb[:, 0, :], x_t[bass.ds(g, 1)].rearrange("o p n -> p (o n)")).then_inc(gx_in, 16)
                    sp.wait_ge(gout_ready, g + 1)
                    sp.dma_start(out[bass.ds(g, 1)].rearrange("o p n -> p (o n)"), out_sb[:, 0, :])\
                        .then_inc(gout_st, 16)

            general(sp, general_pair, stores=(gout_st,))

        @block.gpsimd
        def _(pool):
            def load_adj(q):
                if q.exists():
                    await_count(pool, loop_done, q.number - RING + 2)
                    await_count(pool, seen_done, q.pair - 1)
                    pool.dma_start(adj_sb[:, q.spot:q.spot + 2, :],
                                   adj[bass.ds(q.pair, 1)].rearrange("o p (g n) -> p (o g) n", g=2))\
                        .then_inc(adj_in[q.spot // 2], 16)

            def load_adjt(q):
                if q.exists():
                    await_count(pool, msg_done, q.number - RING + 2)
                    pool.dma_start(adjt_sb[:, q.spot:q.spot + 2, :],
                                   adj_t[bass.ds(q.pair, 1)].rearrange("o p (g n) -> p (o g) n", g=2))\
                        .then_inc(adjt_in[q.spot // 2], 16)

            def norm1(q):
                if q.exists():
                    pool.wait_ge(tiny_done, (q.pair + 1) * STAT_OPS)
                    await_count(pool, z_done, q.number - RING + 1)
                    nc.gpsimd.tensor_tensor(ticket[:, 1 + q.spot:2 + q.spot], ticket[:, 0:1], ticket[:, 0:1], ALU.add)
                    par = q.spot // 2
                    for b in range(GB):
                        c = q.spot % 2 * GB + b
                        last = nc.gpsimd.tensor_scalar(
                            x1[:, q.spot, batch(b)], s_sb[:, q.spot, batch(b)], rstd[:, par, 0, c:c + 1],
                            nmr[:, par, 0, c:c + 1], ALU.mult, ALU.add)
                    last.then_inc(x1_done, 1)

            nc.gpsimd.memset(ticket[:, :], 0.0).then_inc(ticket_ready, 1)
            pool.wait_ge(ticket_ready, 1)
            load_adj(Group(0, 0))

            def slot(t):
                if t.offset % 2 == 0:
                    load_adjt(t.back(4))
                elif not t.fixed or t.number + 2 < GROUPS:
                    load_adj(t.back(-1))
                norm1(t.back(LAG_NORM1))

            full = FULL
            for t in range(full):
                slot(Group(t // RING, t % RING))
            with pool.Fori(full // RING, GROUPS // RING - 1) as period:
                for j in range(RING):
                    slot(Group(period, j))
            for t in range(GROUPS - RING, SLOTS):
                slot(Group(t // RING, t % RING))

            def general_pair(pair):
                pool.dma_start(adj_sb[:, 0:2, :], adj[bass.ds(pair, 1)].rearrange("o p (g n) -> p (o g) n", g=2))\
                    .then_inc(gadj_in, 16)
                pool.dma_start(adjt_sb[:, 0:2, :], adj_t[bass.ds(pair, 1)].rearrange("o p (g n) -> p (o g) n", g=2))\
                    .then_inc(gadj_in, 16)
                pool.wait_ge(gout_ready, pair * 2 + 2)

            general(pool, general_pair)

        @block.tensor
        def _(pe):
            pe.wait_ge(fold_in, 16 * 2)
            nc.tensor.matmul(msg_ps[:, 0:P], w_loop[:, :], wg_t[:, :], start=True, stop=True).then_inc(fold_done, 1)
            pe.wait_ge(weights_ready, 2)
            pe.wait_ge(w_in_sem, 16 * 2)

            def project(q):
                if q.exists():
                    pe.wait_ge(xt_in[q.spot], 16 * (q.turn + 1))
                    await_count(pe, vals_done, q.number - 1)
                    buf = q.spot % 2
                    for half in range(2):
                        nc.tensor.matmul(hg_ps[:, buf, 2 * half:2 * half + 2, :], pick_r[:, :], b_split[:, 0, :],
                                         start=True, stop=False, skip_group_check=True)
                        for b in (2 * half, 2 * half + 1):
                            last = nc.tensor.matmul(hg_ps[:, buf, b, :], xt_sb[:, q.spot, batch(b)], w_gate[:, :],
                                                    start=False, stop=b % 2 == 1, skip_group_check=True)
                    last.then_inc(hg_done, 1)

            def loop_sum(q):
                if q.exists():
                    pe.wait_ge(adj_in[q.spot // 2], 16 * (q.turn + 1))
                    pe.wait_ge(vals_done, q.number + 1)
                    await_count(pe, s_done, q.number - 1)
                    buf = q.spot % 2
                    for b in range(GB):
                        last = nc.tensor.matmul(loop_ps[:, buf, batch(b)], adj_sb[:, q.spot, batch(b)],
                                                vals[:, buf, batch(b)], start=True, stop=True)
                    last.then_inc(loop_done, 1)

            def messages(q):
                if q.exists():
                    pe.wait_ge(adjt_in[q.spot // 2], 16 * (q.turn + 1))
                    pe.wait_ge(x1_done, q.number + 1)
                    await_count(pe, msgt_done, q.number)
                    for b in range(GB):
                        last = nc.tensor.matmul(msg_ps[:, batch(b)], x1[:, q.spot, batch(b)],
                                                adjt_sb[:, q.spot, batch(b)], start=True, stop=True)
                    last.then_inc(msg_done, 1)

            def message_weights(q):
                if q.exists():
                    pe.wait_ge(msgt_done, q.number + 1)
                    await_count(pe, z_done, q.number)
                    nc.tensor.matmul(y_ps[:, :], pick_r[:, :], b_split[:, 1, :], start=True, stop=False,
                                     skip_group_check=True)
                    for b in range(GB):
                        last = nc.tensor.matmul(y_ps[:, batch(b)], msg_t[:, q.spot % 2, batch(b)], w1[:, :],
                                                start=False, stop=b == GB - 1, skip_group_check=True)
                    last.then_inc(y_done, 1)

            def slot(t):
                late = t.fixed and t.number >= GROUPS
                if not late:
                    project(t)
                loop_sum(t.back(LAG_LOOP))
                messages(t.back(LAG_MSG))
                message_weights(t.back(LAG_PROJ))
                if t.fixed and t.number == GROUPS + 1:
                    pe.wait_ge(odd_ready, 2)
                    pe.wait_ge(vals_done, GROUPS)
                    nc.tensor.matmul(hg_ps[0:1, 0, 0, 0:1], odd[:, :], ones[:, :], start=True, stop=True)\
                        .then_inc(odd_count, 1)

            run_slots(pe, slot)

            def relation(step, ways):
                pe.wait_ge(rel_vals, step)
                for way in ways:
                    for b in range(GB):
                        last = nc.tensor.transpose(bank[way][:, batch(b)], gvals_t[:, way, batch(b)], ident[:, :])
                last.then_inc(rel_turned, 1)
                pe.wait_ge(rel_copied, step)
                for b in range(GB):
                    for way in ways:
                        last = nc.tensor.matmul(bank[3][:, batch(b)], gmask[:, way, batch(b)],
                                                gvals[:, way, batch(b)], start=way == ways[0], stop=way == ways[-1])
                last.then_inc(rel_product, 1)

            def general_pair(pair):
                for half in range(2):
                    g = pair * 2 + half
                    pe.wait_ge(gx_in, (g + 1) * 32)
                    for way in (FWD, BWD, LOOP):
                        last = nc.tensor.matmul(bank[way], gw_t[:, way, :], xt_sb[:, 0, :], start=True, stop=True)
                    last.then_inc(gh_done, 1)
                    pe.wait_ge(gh_copied, g + 1)
                    for way in (FWD, BWD, LOOP):
                        last = nc.tensor.matmul(bank[way], gwg_t[:, way, :], gh[:, way, :], start=True, stop=True)
                    last.then_inc(gg_done, 1)
                    first = g * (RELS + 1) + 1
                    relation(first, (BWD,))
                    with pe.Fori(0, RELS) as r:
                        relation(first + 1 + r, (FWD, BWD))
                    pe.wait_ge(gmasks_ready, g + 1)
                    for k in range(MSGS):
                        for b in range(GB):
                            last = nc.tensor.matmul(bank[k][:, batch(b)], gx1[:, batch(b)], gmask[:, k, batch(b)],
                                                    start=True, stop=True)
                    last.then_inc(gmsg_done, 1)
                    pe.wait_ge(gmsg_copied, g + 1)
                    nc.tensor.matmul(y_ps[:, :], pick_r[:, :], b_split[:, 1, :], start=True, stop=False,
                                     skip_group_check=True)
                    for b in range(GB):
                        for k in range(MSGS):
                            last = nc.tensor.matmul(y_ps[:, batch(b)], gmsg[:, k, batch(b)], gw_msg[:, k, :],
                                                    start=False, stop=b == GB - 1 and k == MSGS - 1,
                                                    skip_group_check=True)
                    last.then_inc(gy_done, 1)

            general(pe, general_pair)

        @block.scalar
        def _(act):
            def copy_messages(q):
                if q.exists():
                    act.wait_ge(msg_done, q.number + 1)
                    await_count(act, y_done, q.number - 1)
                    nc.scalar.activation(msg_t[:, q.spot % 2, :], msg_ps[:, :], ACT.Copy).then_inc(msgt_done, 1)

            def norm2(q):
                if q.exists():
                    act.wait_ge(tiny_done, (q.pair + LAG_NORM2 // 2 - 1) * STAT_OPS)
                    await_count(act, out_st[q.spot], 16 * q.turn)
                    par = (q.spot // 2 + LAG_NORM2 // 2) % 2
                    for b in range(GB):
                        c = q.spot % 2 * GB + b
                        last = nc.scalar.activation(out_sb[:, q.spot, batch(b)], z_sb[:, q.spot, batch(b)],
                                                    ACT.Identity, bias=nmr[:, par, 1, c:c + 1],
                                                    scale=rstd[:, par, 1, c:c + 1])
                    last.then_inc(out_done, 1)

            def look(q):
                if q.exists():
                    act.wait_ge(adj_in[q.spot // 2], 16 * (q.turn + 1))
                    await_count(act, seen_done, q.pair)
                    nc.scalar.activation(seen[:, :], adj_sb[:, q.spot:q.spot + 2, :].rearrange("p g n -> p (g n)"),
                                         ACT.Square, bias=half[:, 0:1],
                                         accum_out=seen_sum[:, bass.ds(q.pair, 1)]).then_inc(seen_done, 1)

            def gates(q):
                if q.exists():
                    act.wait_ge(hg_done, q.number + 1)
                    await_count(act, vals_done, q.number - 1)
                    nc.scalar.activation(gate[:, q.spot % 2, :].rearrange("p (b n) -> p b n", b=GB),
                                         hg_ps[:, q.spot % 2, :, P:2 * P], ACT.Sigmoid).then_inc(gate_done, 1)

            act.wait_ge(const_ready, 3)

            def slot(t):
                late = t.fixed and t.number >= GROUPS
                if not late:
                    gates(t)
                copy_messages(t.back(LAG_MSG))
                norm2(t.back(LAG_NORM2))
                if not late and t.offset % 2 == 0:
                    look(t)

            run_slots(act, slot)

            def copy_turned(step, ways):
                act.wait_ge(rel_turned, step)
                for way in ways:
                    last = nc.scalar.activation(gvals[:, way, :], bank[way], ACT.Copy)
                last.then_inc(rel_copied, 1)

            def general_pair(pair):
                for half in range(2):
                    g = pair * 2 + half
                    act.wait_ge(gh_done, g + 1)
                    for way in (FWD, BWD, LOOP):
                        last = nc.scalar.activation(gh[:, way, :], bank[way], ACT.Copy)
                    last.then_inc(gh_copied, 1)
                    act.wait_ge(gg_done, g + 1)
                    for way in (FWD, BWD):
                        nc.scalar.activation(gg[:, way, :], bank[way], ACT.Copy).then_inc(gg_copied, 1)
                    nc.scalar.activation(ggate[:, BWD, :], bank[LOOP], ACT.Sigmoid,
                                         bias=gbg[:, 2 * RELS:2 * RELS + 1]).then_inc(rel_gates, 1)
                    act.wait_ge(gg_copied, g * 2 + 2)
                    first = g * (RELS + 1) + 1
                    copy_turned(first, (BWD,))
                    with act.Fori(0, RELS) as r:
                        act.wait_ge(rel_added, first + r)
                        for way in (FWD, BWD):
                            last = nc.scalar.activation(ggate[:, way, :], gg[:, way, :], ACT.Sigmoid,
                                                        bias=gbg[:, bass.ds(r + way * RELS, 1)])
                        last.then_inc(rel_gates, 1)
                        copy_turned(first + 1 + r, (FWD, BWD))
                    act.wait_ge(gmsg_done, g + 1)
                    for k in range(MSGS):
                        last = nc.scalar.activation(gmsg[:, k, :], bank[k], ACT.Copy)
                    last.then_inc(gmsg_copied, 1)

            general(act, general_pair)

        @block.vector
        def _(dve):
            nc.vector.memset(b_rows[:, :, :], 0.0).then_inc(cleared, 1)
            nc.vector.memset(pick[:, :], 0.0).then_inc(const_ready, 1)
            nc.vector.memset(half[:, :], -0.5).then_inc(const_ready, 1)
            nc.vector.memset(stats[:, :, :, :, :].rearrange("p a b c d -> p (a b c d)"), 0.0).then_inc(const_ready, 1)
            nc.vector.memset(ones[:, :], 1.0)
            dve.wait_ge(const_ready, 3)
            nc.vector.memset(pick[0:1, :], 1.0)
            nc.vector.memset(pick[32:33, :], 1.0).then_inc(const_ready, 1)
            dve.wait_ge(const_ready, 4)
            nc.vector.tensor_copy(pick_r[:, :], pick[:, :])
            dve.wait_ge(bias_in, 16 * 2)
            nc.vector.tensor_copy(b_split[:, :, :], b_rows[:, :, :]).then_inc(const_ready, 1)
            dve.wait_ge(const_ready, 5)
            nc.vector.tensor_tensor(b_split[32:33, :, :], b_rows[32:33, :, :], b_split[32:33, :, :].bitcast(F32),
                                    ALU.subtract).then_inc(weights_ready, 1)
            dve.wait_ge(fold_done, 1)
            nc.vector.tensor_copy(w_gate[:, P:2 * P], msg_ps[:, 0:P]).then_inc(weights_ready, 1)

            def statistics(t):
                par = (t.offset - FIRST_STATS) // 2 % 2
                st = stats[:, par, :, :, :]
                done = (t.back(FIRST_STATS).pair) * STAT_OPS
                add, diff, m2, var, y, yy, w = (tiny[:, i, :, :] for i in range(7))
                r, n = rstd[:, par, :, :], nmr[:, par, :, :]
                tt, ts, stt = nc.vector.tensor_tensor, nc.vector.tensor_scalar, nc.vector.scalar_tensor_tensor
                steps = [
                    lambda: tt(add, st[:, :, :, 1], st[:, :, :, 4], ALU.add),
                    lambda: tt(diff, st[:, :, :, 1], st[:, :, :, 4], ALU.subtract),
                    lambda: tt(m2, st[:, :, :, 2], st[:, :, :, 5], ALU.add),
                    lambda: stt(w, diff, P / 4.0, diff, ALU.mult, ALU.mult),
                    lambda: tt(m2, m2, w, ALU.add),
                    lambda: ts(var, m2, 1.0 / P, EPS, ALU.mult, ALU.add),
                    lambda: ts(y.bitcast(I32), var.bitcast(I32), -0.5, RSQRT_MAGIC, ALU.mult, ALU.add),
                ]
                for k in range(NEWTON):
                    steps += [
                        lambda: tt(yy, y, y, ALU.mult),
                        lambda: stt(w, yy, -0.5, var, ALU.mult, ALU.mult),
                        lambda k=k: stt(r if k == NEWTON - 1 else y, w, 1.5, y, ALU.add, ALU.mult),
                    ]
                steps.append(lambda: stt(n, add, -0.5, r, ALU.mult, ALU.mult))
                assert len(steps) == STAT_OPS
                for k, step in enumerate(steps):
                    if k == 0:
                        await_count(dve, bn1_done, t.back(2).count)
                        await_count(dve, bn2_done, t.back(LAG_NORM2 - 2).count)
                        await_count(dve, x1_done, t.back(FIRST_STATS + 3).count)
                        await_count(dve, out_done, t.back(LAG_NORM2 + 2).count)
                    await_count(dve, tiny_done, done + k)
                    step().then_inc(tiny_done, 1)
                    yield

            def values(q):
                if q.exists():
                    dve.wait_ge(gate_done, q.number + 1)
                    await_count(dve, loop_done, q.number - 1)
                    nc.vector.tensor_tensor(vals[:, q.spot % 2, :].rearrange("p (b n) -> p b n", b=GB),
                                            hg_ps[:, q.spot % 2, :, 0:P],
                                            gate[:, q.spot % 2, :].rearrange("p (b n) -> p b n", b=GB),
                                            ALU.mult).then_inc(vals_done, 1)
                    yield

            def first_sum(q):
                if q.exists():
                    dve.wait_ge(loop_done, q.number + 1)
                    dve.wait_ge(x_in[q.spot], 16 * (q.turn + 1))
                    await_count(dve, x1_done, q.number - RING + 1)
                    nc.vector.scalar_tensor_tensor(s_sb[:, q.spot, :], loop_ps[:, q.spot % 2, :], 0.0,
                                                   x_sb[:, q.spot, :], ALU.max, ALU.add).then_inc(s_done, 1)
                    yield
                    dve.wait_ge(s_done, q.number + 1)
                    for b in range(GB):
                        last = nc.vector.bn_stats(stats[:, q.spot // 2, 0, q.spot % 2 * GB + b, :],
                                                  s_sb[:, q.spot, batch(b)])
                        if b < GB - 1:
                            yield
                    last.then_inc(bn1_done, 1)
                    yield

            def second_sum(q):
                if q.exists():
                    dve.wait_ge(y_done, q.number + 1)
                    dve.wait_ge(x1_done, q.number + 1)
                    await_count(dve, out_done, q.number - RING + 1)
                    nc.vector.tensor_tensor(z_sb[:, q.spot, :], y_ps[:, :], x1[:, q.spot, :],
                                            ALU.add).then_inc(z_done, 1)
                    yield
                    dve.wait_ge(z_done, q.number + 1)
                    for b in range(GB):
                        last = nc.vector.bn_stats(stats[:, (q.spot // 2 + LAG_NORM2 // 2) % 2, 1, q.spot % 2 * GB + b, :],
                                                  z_sb[:, q.spot, batch(b)])
                        if b < GB - 1:
                            yield
                    last.then_inc(bn2_done, 1)
                    yield

            def find_odd():
                dve.wait_ge(seen_done, GROUPS // 2)
                nc.vector.tensor_reduce(worst[:, :], seen_sum[:, :], AX_X, ALU.max).then_inc(odd_ready, 1)
                dve.wait_ge(odd_ready, 1)
                nc.vector.tensor_scalar(odd[:, :], worst[:, :], 2 * W / 4 + 0.5, None, ALU.is_gt)\
                    .then_inc(odd_ready, 1)

            def slot(t):
                small = iter(())
                if t.offset % 2 == 1 and (not t.fixed or t.number >= FIRST_STATS):
                    small = statistics(t)
                late = t.fixed and t.number >= GROUPS
                for _ in range(6):
                    next(small, None)
                for large in (() if late else values(t), first_sum(t.back(LAG_LOOP)), second_sum(t.back(LAG_PROJ))):
                    for _ in large:
                        next(small, None)
                for _ in small:
                    pass
                if t.fixed and t.number == GROUPS:
                    find_odd()

            run_slots(dve, slot)
            dve.wait_ge(odd_count, 1)
            nc.vector.tensor_copy(flag[:, :], hg_ps[0:1, 0, 0, 0:1]).then_inc(flag_ready, 1)

            def vals_and_masks(step, half, ways, r, number):
                dve.wait_ge(rel_gates, step)
                for way in ways:
                    source = LOOP if r is None else way
                    column = bass.ds(2 * RELS if r is None else r + way * RELS, 1)
                    nc.vector.scalar_tensor_tensor(gvals_t[:, way, :], gh[:, source, :], gb[:, column],
                                                   ggate[:, way, :], ALU.add, ALU.mult)
                for way in ways:
                    edges = adjt_sb[:, half, :] if way == FWD else adj_sb[:, half, :]
                    last = nc.vector.tensor_scalar(gmask[:, way, :], edges, number, None, ALU.is_equal)
                last.then_inc(rel_vals, 1)

            def normalise(dst, src, chain):
                var, y, yy, w = (gtiny[:, i, :] for i in range(4))
                for b in range(GB):
                    last = nc.vector.bn_stats(gstat[:, b, :], src[:, batch(b)])
                chain(last)
                nc.vector.tensor_copy(worst[:, :], ones[:, :])
                for b in range(GB):
                    last = nc.vector.bn_aggr(gmv[:, b, :], gstat[:, b, :])
                chain(last)
                chain(nc.vector.tensor_scalar(var, gmv[:, :, 1], EPS, None, ALU.add))
                chain(nc.vector.tensor_scalar(y.bitcast(I32), var.bitcast(I32), -0.5, RSQRT_MAGIC,
                                              ALU.mult, ALU.add))
                for _ in range(NEWTON):
                    chain(nc.vector.tensor_tensor(yy, y, y, ALU.mult))
                    chain(nc.vector.scalar_tensor_tensor(w, yy, -0.5, var, ALU.mult, ALU.mult))
                    chain(nc.vector.scalar_tensor_tensor(y, w, 1.5, y, ALU.add, ALU.mult))
                for b in range(GB):
                    last = nc.vector.tensor_scalar(dst[:, batch(b)], src[:, batch(b)], gmv[:, b, 0:1], y[:, b:b + 1],
                                                   ALU.subtract, ALU.mult)
                chain(last)

            def general_pair(pair):
                dve.wait_ge(gadj_in, (pair + 1) * 32)
                for half in range(2):
                    g = pair * 2 + half
                    steps = [0]

                    def chain(ins):
                        steps[0] += 1
                        ins.then_inc(gchain, 1)
                        dve.wait_ge(gchain, g * CHAIN + steps[0])

                    first = g * (RELS + 1) + 1
                    vals_and_masks(first, half, (BWD,), None, 1.0)
                    dve.wait_ge(rel_product, first)
                    nc.vector.tensor_copy(gsum[:, :], bank[3]).then_inc(rel_added, 1)
                    with dve.Fori(0, RELS) as r:
                        vals_and_masks(first + 1 + r, half, (FWD, BWD), r, gids[:, bass.ds(r, 1)])
                        dve.wait_ge(rel_product, first + 1 + r)
                        nc.vector.tensor_tensor(gsum[:, :], bank[3], gsum[:, :], ALU.add).then_inc(rel_added, 1)
                    dve.wait_ge(rel_added, first + RELS)
                    dve.wait_ge(gx_in, (g + 1) * 32)
                    chain(nc.vector.scalar_tensor_tensor(gsum[:, :], gsum[:, :], 0.0, x_sb[:, 0, :],
                                                         ALU.max, ALU.add))
                    normalise(gx1, gsum, chain)
                    for k in range(MSGS):
                        last = nc.vector.tensor_scalar(gmask[:, k, :], adjt_sb[:, half, :], float(k + 1),
                                                       None, ALU.is_equal)
                    last.then_inc(gmasks_ready, 1)
                    dve.wait_ge(gy_done, g + 1)
                    chain(nc.vector.tensor_tensor(gsum[:, :], y_ps[:, :], gx1[:, :], ALU.add))
                    normalise(out_sb[:, 0, :], gsum, chain)
                    assert steps[0] == CHAIN
                    nc.vector.tensor_copy(worst[:, :], ones[:, :]).then_inc(gout_ready, 1)
                    dve.wait_ge(gout_st, (g + 1) * 16)

            general(dve, general_pair)


_OUT_SHAPE = (128, 128, 128)


def kernel(**inputs):
    import numpy as _np
    import concourse.bacc as _bacc
    from concourse import mybir as _mybir
    from concourse.bass_utils import run_bass_kernel_spmd as _run

    def grouped(a, per):
        n = a.shape[0] // per
        return _np.ascontiguousarray(a.reshape(n, per, P, P).transpose(0, 2, 1, 3)).reshape(n, P, per * P)

    x = _np.asarray(inputs["x"])
    adj = _np.asarray(inputs["adj"])
    w = {k: _np.asarray(v) for k, v in inputs.items()}
    gate_bias = _np.concatenate([w["L0_gnn_b_loop"], w["L0_gnn_bg_loop"]], axis=1)
    arrays = {
        "x": grouped(x, GB),
        "x_t": grouped(x.transpose(0, 2, 1), GB),
        "adj": grouped(adj, 2 * GB),
        "adj_t": grouped(adj.transpose(0, 2, 1), 2 * GB),
        "w_loop": _np.ascontiguousarray(w["L0_gnn_W_loop"]),
        "w_loop_t": _np.ascontiguousarray(w["L0_gnn_W_loop"].T),
        "wg_loop_t": _np.ascontiguousarray(w["L0_gnn_Wg_loop"].T),
        "biases": _np.concatenate([gate_bias, gate_bias] + [w["L1_gnn_bias"][None]] * GB, axis=1).reshape(1, 2, W),
        "w_msg": _np.ascontiguousarray(w["L1_gnn_weight"][0]),
    }
    ways = ("fwd", "bwd", "loop")
    arrays.update({
        "w_rel_t": _np.stack([w[f"L0_gnn_W_{k}"].T for k in ways], axis=1),
        "wg_rel_t": _np.stack([w[f"L0_gnn_Wg_{k}"].T for k in ways], axis=1),
        "b_rel": _np.ascontiguousarray(_np.concatenate([w[f"L0_gnn_b_{k}"].T for k in ways], axis=1)),
        "bg_rel": _np.ascontiguousarray(_np.concatenate([w[f"L0_gnn_bg_{k}"].T for k in ways], axis=1)),
        "w_msgs": _np.ascontiguousarray(w["L1_gnn_weight"].transpose(1, 0, 2)),
        "rel_ids": _np.tile(_np.arange(2, 2 + RELS, dtype=_np.float32), (P, 1)),
        "identity": _np.eye(P, dtype=_np.float32),
    })
    nc = _bacc.Bacc("TRN2", target_bir_lowering=False, num_devices=1)
    args = [nc.dram_tensor(n + "_dram", a.shape, _mybir.dt.from_np(a.dtype), kind="ExternalInput").ap()
            for n, a in arrays.items()]
    out = nc.dram_tensor("out", (GROUPS, P, W), F32, kind="ExternalOutput").ap()
    build(nc, *args, out)
    r = _run(nc, [{n + "_dram": a for n, a in arrays.items()}], core_ids=[0])
    y = r.results[0]["out"]
    return y.reshape(GROUPS, P, GB, P).transpose(0, 2, 1, 3).reshape(_OUT_SHAPE)
```
